# Optimizing a Trainium2 kernel written in Bass

```python
import numpy as np
import jax
import jax.numpy as jnp

def _softmax(x, axis=-1):
    return jax.nn.softmax(x, axis=axis)

def _gelu(x):
    return jax.nn.gelu(x, approximate=True)

def _silu(x):
    return jax.nn.silu(x)

def _sigmoid(x):
    return jax.nn.sigmoid(x)

def _layernorm(x, axis=-1, eps=1e-05):
    m = jnp.mean(x, axis=axis, keepdims=True)
    v = jnp.var(x, axis=axis, keepdims=True)
    return (x - m) / jnp.sqrt(v + eps)

def _scatter_add(tgt, idx, src, axis=0):
    return tgt.at[idx].add(src)

def _segment_sum(src, seg, n):
    return jax.ops.segment_sum(src, seg, n)
kernel_name = 'mk_prb_d1_jaxref_r4_941c3d'

def setup_inputs(seed: int=0):
    np.random.seed(seed)
    _w = jnp.asarray

    def _L0_attn_setup():
        import jax, jax.numpy as jnp
        import numpy as np
        DIM = 256
        HEADS = 16
        HEAD_DIM = DIM // HEADS

        def _xavier(key, shape):
            fan_out, fan_in = shape
            limit = float(np.sqrt(6.0 / (fan_in + fan_out)))
            return jax.random.uniform(key, shape, jnp.float32, -limit, limit)
        key = jax.random.key(seed)
        kx, kv, kk, kq = jax.random.split(key, 4)
        x = jax.random.normal(kx, (4, 512, DIM), jnp.float32)
        Wv = _xavier(kv, (DIM, DIM))
        Wk = _xavier(kk, (DIM, DIM))
        Wq = _xavier(kq, (DIM, DIM))
        return {'x': x, 'Wq': Wq, 'Wk': Wk, 'Wv': Wv}
    _L0_attn_in = _L0_attn_setup()

    def _L0_ffn_setup():
        import jax, jax.numpy as jnp
        import numpy as np
        EPS = 1e-05

        def _quantize(W):
            gamma = jnp.mean(jnp.abs(W))
            return jnp.clip(jnp.round(W / (gamma + EPS)), -1.0, 1.0)
        key = jax.random.key(seed)
        k_x, k_w1, k_b1, k_w2, k_b2 = jax.random.split(key, 5)
        n_embd = 256
        d_ff = 4 * n_embd
        B, S = (4, 1024)
        bound1 = 1.0 / np.sqrt(n_embd)
        bound2 = 1.0 / np.sqrt(d_ff)
        x = jax.random.normal(k_x, (B, S, n_embd), dtype=jnp.float32)
        W1 = jax.random.uniform(k_w1, (d_ff, n_embd), jnp.float32, -bound1, bound1)
        b1 = jax.random.uniform(k_b1, (d_ff,), jnp.float32, -bound1, bound1)
        W2 = jax.random.uniform(k_w2, (n_embd, d_ff), jnp.float32, -bound2, bound2)
        b2 = jax.random.uniform(k_b2, (n_embd,), jnp.float32, -bound2, bound2)
        return {'x': x, 'W1': W1, 'b1': b1, 'W2': W2, 'b2': b2}
    _L0_ffn_in = _L0_ffn_setup()
    _d = {'L0_attn_x': _L0_attn_in['x'], 'L0_attn_Wq': _L0_attn_in['Wq'], 'L0_attn_Wk': _L0_attn_in['Wk'], 'L0_attn_Wv': _L0_attn_in['Wv'], 'L0_ffn_W1': _L0_ffn_in['W1'], 'L0_ffn_b1': _L0_ffn_in['b1'], 'L0_ffn_W2': _L0_ffn_in['W2'], 'L0_ffn_b2': _L0_ffn_in['b2']}
    _x0 = _d['L0_attn_x']
    _d['L0_attn_x'] = jax.random.normal(jax.random.fold_in(jax.random.key(seed), 1), (8, 1024, 256), dtype=_x0.dtype)
    del _x0
    return _d

def reference(L0_attn_x, L0_attn_Wq, L0_attn_Wk, L0_attn_Wv, L0_ffn_W1, L0_ffn_b1, L0_ffn_W2, L0_ffn_b2):

    def _L0_attn_ref(x, Wq, Wk, Wv):
        import jax, jax.numpy as jnp
        import numpy as np
        DIM = 256
        HEADS = 16
        HEAD_DIM = DIM // HEADS

        def _xavier(key, shape):
            fan_out, fan_in = shape
            limit = float(np.sqrt(6.0 / (fan_in + fan_out)))
            return jax.random.uniform(key, shape, jnp.float32, -limit, limit)
        B, S, D = x.shape
        H, Hd = (HEADS, HEAD_DIM)
        q = (x @ Wq.T).reshape(B, S, H, Hd)
        k = (x @ Wk.T).reshape(B, S, H, Hd)
        v = (x @ Wv.T).reshape(B, S, H, Hd)
        energy = jnp.einsum('bqhd,bkhd->bhqk', q, k)
        attn = jax.nn.softmax(energy / jnp.sqrt(jnp.float32(D)), axis=-1)
        out = jnp.einsum('bhqk,bkhd->bqhd', attn, v).reshape(B, S, D)
        return out

    def _L0_ffn_ref(x, W1, b1, W2, b2):
        import jax, jax.numpy as jnp
        import numpy as np
        EPS = 1e-05

        def _quantize(W):
            gamma = jnp.mean(jnp.abs(W))
            return jnp.clip(jnp.round(W / (gamma + EPS)), -1.0, 1.0)
        Wq1 = _quantize(W1)
        Wq2 = _quantize(W2)
        h = jax.nn.relu(jnp.einsum('bsd,fd->bsf', x, Wq1) + b1)
        out = jnp.einsum('bsf,df->bsd', h, Wq2) + b2
        return out
    x = L0_attn_x
    xn = _layernorm(x, axis=-1)
    x = x + _L0_attn_ref(xn, L0_attn_Wq, L0_attn_Wk, L0_attn_Wv) + _L0_ffn_ref(xn, L0_ffn_W1, L0_ffn_b1, L0_ffn_W2, L0_ffn_b2)
    return x

_drawn_inputs = setup_inputs


def setup_inputs(seed=0):
    import zlib

    import numpy as np

    out = dict(_drawn_inputs(seed))
    spreads = {}
    factors = {'L0_attn_Wq': 8.0,
     'L0_attn_Wk': 8.0,
     'L0_attn_Wv': 8.0,
     'L0_ffn_b1': 22.155,
     'L0_ffn_b2': 64.0}
    for name, (base, spread) in spreads.items():
        noise = np.random.default_rng([zlib.crc32(name.encode()), seed]).standard_normal(out[name].shape)
        drawn = base * np.exp(spread * noise) if base else spread * noise
        out[name] = jnp.asarray(drawn.astype(out[name].dtype))
    for name, factor in factors.items():
        out[name] = (out[name] * factor).astype(out[name].dtype)
    return out
```

```python
import itertools
from contextlib import ExitStack

import concourse.bass as bass
from concourse import mybir

F32 = mybir.dt.float32
F32R = mybir.dt.float32r
ALU = mybir.AluOpType
ACT = mybir.ActivationFunctionType
AX_X = mybir.AxisListType.X

P = 128
BANK = 512
EPS = 1e-05

B, S, D = 8, 1024, 256
H, HD = 16, 16
FF = 4 * D
DH = D // P
FT = FF // P
BLK = 512
TB = BLK // P
NT = S // P
MT = 2 * D // P
PAIRS = B * H // 2
VC = HD + 1
UN = 4
NIT = PAIRS // UN
LN = 9
V_BANK = (6, 7, 4, 5)
LEAD = 4
STEPS = NT
SLOTS = 4 * STEPS
NS = 3
NP = 4
QROWS = 3 * HD
MROW = 96
CR = MROW + 2


REGISTERS = itertools.count()


def register(eng):
    return eng.alloc_register(f"count{next(REGISTERS)}")


class Turn:

    def __init__(self, eng, it, multiples):
        self.at = it
        self.times = {}
        for m in sorted(multiples):
            self.times[m] = register(eng)
            eng.reg_mul(self.times[m], eng.to_reg(it), m)


def at(it):
    return it if isinstance(it, int) else it.at


def wait_all(eng, *waits):
    values = []
    for sem, it, per, add in waits:
        if not isinstance(it, int):
            value = it.times[per]
            if add:
                value = register(eng)
                eng.reg_add(value, it.times[per], add)
            values.append((sem, value))
        elif per * it + add > 0:
            values.append((sem, per * it + add))
    for sem, value in values:
        eng.wait_ge(sem, value)


def wait(eng, sem, it, per, add):
    wait_all(eng, (sem, it, per, add))


def looped(eng, n, multiples, body):
    body(0, True, False)
    with eng.Fori(1, n - 1) as it:
        body(Turn(eng, it, multiples), False, False)
    body(n - 1, False, True)


def part_a(nc, x, wqkt, wvt, w1t, w2t, b1t, b2, qk_d, v_d, Y, ident):
    with ExitStack() as ctx:
        def sb(name, shape, dt=F32):
            return ctx.enter_context(nc.sbuf_tensor(name, shape, dt))

        def sem(name):
            return ctx.enter_context(nc.semaphore(name))

        ps = ctx.enter_context(nc.psum_tensor("psA", [P, 8, BANK], F32))
        wqk_raw = sb("wqk_raw", [P, DH, 2 * D])
        wv_raw = sb("wv_raw", [P, DH, D])
        wf_raw = sb("wf_raw", [P, 2, 1024])
        mag = sb("mag", [P, 1024])
        part_sum = sb("part_sum", [P, 4])
        thresh = sb("thresh", [P, 4])
        ones = sb("ones", [P, P])
        wqk = [sb("wqk_hi", [P, DH, 2 * D], F32R), sb("wqk_lo", [P, DH, 2 * D], F32R)]
        wv = [sb("wv_hi", [P, DH, D], F32R), sb("wv_lo", [P, DH, D], F32R)]
        w1q = sb("w1q", [P, DH, FF], F32R)
        w2q = sb("w2q", [P, FT, D], F32R)
        b1c = sb("b1c", [P, FT])
        b2b = sb("b2b", [P, D])
        xin = sb("xin", [P, 2, TB, D])
        xn = sb("xn", [P, TB, D])
        stats = sb("stats", [P, TB, 6])
        pair = sb("pair", [P, TB, 2])
        diff = sb("diff", [P, TB])
        mean = sb("mean", [P, TB])
        var = sb("var", [P, TB])
        root = sb("root", [P, TB])
        tmp = sb("tmp", [P, TB])
        rstd = sb("rstd", [P, TB])
        xt = [sb("xt_hi", [P, DH, BLK], F32R), sb("xt_lo", [P, DH, BLK], F32R)]
        qk_st = sb("qk_st", [P, MT, 2, BLK], F32R)
        v_st = sb("v_st", [P, 2, H // 2, TB, 2 * VC])
        hf = sb("hf", [P, 4, BLK])
        hh = sb("hh", [P, FT, BLK], F32R)
        hl = sb("hl", [P, FT, BLK], F32R)

        qk_a = qk_d.rearrange("s (b m h) r d t -> s b m h r d t", b=B, m=DH)
        v_a = v_d.rearrange("(b a) p t c -> b a p t c", b=B)

        w_loaded = [sem(f"w_loaded{i}") for i in range(5)]
        x_loaded = [sem("x_loaded0"), sem("x_loaded1")]
        consts_set = sem("consts_set")
        ident_set = sem("ident_set")
        dve_chain = sem("dve_chain")
        sums_ready = sem("sums_ready")
        total_ready = sem("total_ready")
        w2_loaded = sem("w2_loaded")
        w_split = sem("w_split")
        w_ternary = sem("w_ternary")
        ln_step = sem("ln_step")
        var_ready = sem("var_ready")
        root_ready = sem("root_ready")
        xn_ready = sem("xn_ready")
        xt_mm = sem("xt_mm")
        xt_hi_ready = sem("xt_hi_ready")
        xt_lo_ready = sem("xt_lo_ready")
        ffn1_mm = sem("ffn1_mm")
        h_ready = sem("h_ready")
        hl_ready = sem("hl_ready")
        qk_mm = sem("qk_mm")
        qk_hi_ready = sem("qk_hi_ready")
        qk_lo_ready = sem("qk_lo_ready")
        v_mm = sem("v_mm")
        v_ready = sem("v_ready")
        xb_ready = sem("xb_ready")
        y_mm = sem("y_mm")
        y_ready = sem("y_ready")
        qk_stored = [sem(f"qk_stored{m}") for m in range(MT)]
        v_stored = [sem("v_stored0"), sem("v_stored1")]

        def y_tile(it, u, t):
            yt = Y[:, bass.ds(2 * at(it), 2), u * TB + t, :]
            return yt

        block = ctx.enter_context(nc.Block())

        @block.sync
        def _(sp):
            def load_x(b, u):
                src = x[bass.ds(b, 1), u * BLK:(u + 1) * BLK, :].rearrange("o (t p) d -> p (o t) d", p=P)
                sp.dma_start(xin[:, u, :, :], src).then_inc(x_loaded[u], 16)

            load_x(0, 0)
            sp.dma_start(wqk_raw[:], wqkt.rearrange("(h p) n -> p h n", p=P)).then_inc(w_loaded[0], 16)
            sp.dma_start(wf_raw[:], w1t.rearrange("(h p) n -> p h n", p=P)).then_inc(w_loaded[1], 16)
            sp.dma_start(wv_raw[:], wvt.rearrange("(h p) n -> p h n", p=P)).then_inc(w_loaded[2], 16)
            sp.dma_start(b1c[:], b1t).then_inc(w_loaded[3], 16)
            sp.dma_start(b2b[:], b2.partition_broadcast(P)).then_inc(w_loaded[4], 16)
            load_x(0, 1)
            sp.wait_ge(w_ternary, 1)
            sp.dma_start(wf_raw[:].rearrange("p a n -> p (a n)"),
                         w2t.rearrange("(t p) n -> p t n", p=P)).then_inc(w2_loaded, 16)

            def body(it, first, last):
                for u in range(2):
                    for m in range(MT):
                        wait(sp, qk_lo_ready, it, 2 * MT, MT * u + m + 1)
                        heads = P // HD
                        for part in range(2):
                            dst = qk_a[m // DH, bass.ds(at(it), 1), m % DH, :, part, :, u * BLK:(u + 1) * BLK]
                            sp.dma_start(dst.rearrange("o h d t -> (o h) d t"),
                                         qk_st[:, m, part, :].bitcast(F32)).then_inc(qk_stored[m], 16)
                    wait(sp, v_ready, it, 2 * TB, TB * u + TB)
                    sp.dma_start(v_a[bass.ds(at(it), 1), :, :, u * TB:(u + 1) * TB, :].rearrange(
                        "o a p t c -> p (o a) t c"), v_st[:, u]).then_inc(v_stored[u], 16)
                    if not last:
                        wait_all(sp, (xn_ready, it, 2, u + 1), (xb_ready, it, 2, u + 1))
                        load_x(at(it) + 1, u)

            looped(sp, B, {2 * MT, 2 * TB, 2}, body)
            for m in range(MT):
                sp.wait_ge(qk_stored[m], 2 * B * 32)
            for u in range(2):
                sp.wait_ge(v_stored[u], B * 16)

        @block.gpsimd
        def _(pool):
            nc.gpsimd.memset(ident[:], 0.0).then_inc(ident_set, 1)
            nc.gpsimd.memset(ones[:], 1.0).then_inc(consts_set, 1)
            pool.wait_ge(ident_set, 1)
            nc.gpsimd.affine_select(out=ident[:], in_=ident[:], compare_op=ALU.not_equal, fill=1.0, base=0,
                                    pattern=[[-1, P]], channel_multiplier=1).then_inc(ident_set, 1)
            nc.gpsimd.memset(v_st[:], 1.0).then_inc(consts_set, 1)
            pool.wait_ge(w_loaded[4], 16)

            def body(it, first, last):
                for u in range(2):
                    wait(pool, x_loaded[u], it, 16, 16)
                    for t in range(TB):
                        op = nc.gpsimd.tensor_tensor(y_tile(it, u, t),
                                                     xin[:, u, t, :].rearrange("p (h c) -> p h c", h=DH),
                                                     b2b[:].rearrange("p (h c) -> p h c", h=DH), ALU.add)
                    op.then_inc(xb_ready, 1)

            looped(pool, B, {16}, body)

        @block.scalar
        def _(act):
            act.wait_ge(w_loaded[1], 16)
            for h in range(2):
                nc.scalar.activation(mag[:], wf_raw[:, h, :], ACT.Abs,
                                     accum_out=part_sum[:, h:h + 1]).then_inc(sums_ready, 1)
                act.wait_ge(sums_ready, h + 1)
            act.wait_ge(var_ready, 1)
            nc.scalar.activation(root[:], var[:], ACT.Sqrt).then_inc(root_ready, 1)

            def xt_hi(it, u):
                for h in range(DH):
                    wait(act, xt_mm, it, 2 * DH, DH * u + h + 1)
                    nc.scalar.activation(xt[0][:, h, :], ps[:, 6 + h, :], ACT.Copy).then_inc(xt_hi_ready, 1)

            xt_hi(0, 0)
            act.wait_ge(w2_loaded, 16)
            for h in range(2):
                nc.scalar.activation(mag[:], wf_raw[:, h, :], ACT.Abs,
                                     accum_out=part_sum[:, 2 + h:3 + h]).then_inc(sums_ready, 1)
                act.wait_ge(sums_ready, h + 3)
            act.wait_ge(w_loaded[3], 16)
            act.wait_ge(consts_set, 2)

            def body(it, first, last):
                for u in range(2):
                    more = not (last and u == 1)
                    for m in range(MT):
                        for f in range(2 * m, 2 * m + 2):
                            wait(act, ffn1_mm, it, 2 * FT, FT * u + f + 1)
                            wait(act, hl_ready, it, 2 * FT, FT * u + f - 3)
                            bank = ps[:, (f + 2) % 4, :]
                            nc.scalar.activation(hf[:, f % 4, :], bank, ACT.Relu, bias=b1c[:, f:f + 1])
                            nc.scalar.activation(hh[:, f, :], bank, ACT.Relu,
                                                 bias=b1c[:, f:f + 1]).then_inc(h_ready, 1)
                        wait(act, qk_mm, it, 2 * MT, MT * u + m + 1)
                        wait(act, qk_stored[m], it, 64, 32 * u)
                        nc.scalar.activation(qk_st[:, m, 0, :], ps[:, 4 + m % 2, :],
                                             ACT.Copy).then_inc(qk_hi_ready, 1)
                        if m == 0 and more:
                            wait(act, var_ready, it, 2, u + 2)
                            nc.scalar.activation(root[:], var[:], ACT.Sqrt).then_inc(root_ready, 1)
                    for t in range(TB):
                        wait(act, v_mm, it, 2 * TB, TB * u + t + 1)
                        if t == 0:
                            wait(act, v_stored[u], it, 16, 0)
                        nc.scalar.activation(
                            v_st[:, u, :, t, :].rearrange("p a (e c) -> p a e c", e=2)[:, :, :, 0:HD],
                            ps[:, V_BANK[t], 0:D].rearrange("p (a e c) -> p a e c", e=2, c=HD),
                            ACT.Copy).then_inc(v_ready, 1)
                    if more:
                        xt_hi(it, u + 1)

            looped(act, B, {2 * DH, 2 * FT, 2, 2 * MT, 64, 2 * TB, 16}, body)

        @block.vector
        def _(dve):
            chained = [0]

            def link(ins):
                chained[0] += 1
                ins.then_inc(dve_chain, 1)
                dve.wait_ge(dve_chain, chained[0])

            def variances(it, u):
                wait(dve, x_loaded[u % 2], it, 16, 16 * (u // 2) + 16)
                for t in range(TB):
                    op = nc.vector.bn_stats(stats[:, t, :], xin[:, u % 2, t, :])
                op.then_inc(ln_step, 1)
                wait(dve, ln_step, it, 2 * LN, LN * u + 1)
                nc.vector.tensor_tensor(diff[:], stats[:, :, 1], stats[:, :, 4], ALU.subtract)
                nc.vector.tensor_tensor(pair[:], stats[:, :, 1:3], stats[:, :, 4:6],
                                        ALU.add).then_inc(ln_step, 1)
                wait(dve, ln_step, it, 2 * LN, LN * u + 2)
                nc.vector.tensor_tensor(diff[:], diff[:], diff[:], ALU.mult)
                nc.vector.tensor_scalar(mean[:], pair[:, :, 0], 0.5, None, ALU.mult).then_inc(ln_step, 1)
                wait(dve, ln_step, it, 2 * LN, LN * u + 3)
                nc.vector.tensor_scalar(diff[:], diff[:], 0.25, EPS, ALU.mult, ALU.add).then_inc(ln_step, 1)
                wait(dve, ln_step, it, 2 * LN, LN * u + 4)
                nc.vector.scalar_tensor_tensor(var[:], pair[:, :, 1], 1.0 / D, diff[:], ALU.mult,
                                               ALU.add).then_inc(var_ready, 1)

            def norm(it, u):
                wait(dve, root_ready, it, 2, u + 1)
                nc.vector.reciprocal(tmp[:], root[:]).then_inc(ln_step, 1)
                wait(dve, ln_step, it, 2 * LN, LN * u + 5)
                nc.vector.tensor_tensor(tmp[:], var[:], tmp[:], ALU.mult).then_inc(ln_step, 1)
                wait(dve, ln_step, it, 2 * LN, LN * u + 6)
                nc.vector.scalar_tensor_tensor(tmp[:], root[:], 1.0, tmp[:], ALU.mult,
                                               ALU.add).then_inc(ln_step, 1)
                wait(dve, ln_step, it, 2 * LN, LN * u + 7)
                nc.vector.reciprocal(rstd[:], tmp[:]).then_inc(ln_step, 1)
                wait(dve, ln_step, it, 2 * LN, LN * u + 8)
                nc.vector.tensor_scalar(rstd[:], rstd[:], 2.0, None, ALU.mult).then_inc(ln_step, 1)
                wait(dve, ln_step, it, 2 * LN, LN * u + 9)
                wait(dve, xt_mm, it, 2 * DH, DH * u)
                for t in range(TB):
                    op = nc.vector.tensor_scalar(xn[:, t, :], xin[:, u % 2, t, :], mean[:, t:t + 1],
                                                 rstd[:, t:t + 1], ALU.subtract, ALU.mult)
                op.then_inc(xn_ready, 1)

            def xt_lo(it, u):
                for h in range(DH):
                    wait(dve, xt_hi_ready, it, 2 * DH, DH * u + h + 1)
                    nc.vector.tensor_tensor(xt[1][:, h, :], ps[:, 6 + h, :], xt[0][:, h, :].bitcast(F32),
                                            ALU.subtract).then_inc(xt_lo_ready, 1)

            def split(raw, parts):
                link(nc.vector.tensor_copy(parts[0][:], raw[:]))
                nc.vector.tensor_tensor(parts[1][:], raw[:], parts[0][:].bitcast(F32),
                                        ALU.subtract).then_inc(w_split, 1)

            def ternary(n, out):
                dve.wait_ge(total_ready, n + 1)
                c = 2 * n
                link(nc.vector.tensor_reduce(thresh[:, c:c + 1], ps[:, 7, 2 * n:2 * n + 2], AX_X, ALU.add))
                link(nc.vector.tensor_scalar(thresh[:, c:c + 1], thresh[:, c:c + 1], 1.0 / (FF * D), EPS,
                                             ALU.mult, ALU.add))
                link(nc.vector.tensor_scalar(thresh[:, c + 1:c + 2], thresh[:, c:c + 1], -0.5, None, ALU.mult))
                link(nc.vector.tensor_scalar(thresh[:, c:c + 1], thresh[:, c:c + 1], 0.5, None, ALU.mult))
                flat = out[:].rearrange("p a n -> p (a n)")
                for h in range(2):
                    link(nc.vector.tensor_scalar(mag[:], wf_raw[:, h, :], thresh[:, c + 1:c + 2], None, ALU.is_lt))
                    op = nc.vector.scalar_tensor_tensor(flat[:, h * 1024:(h + 1) * 1024], wf_raw[:, h, :],
                                                        thresh[:, c:c + 1], mag[:], ALU.is_gt, ALU.subtract)
                    if h == 0:
                        link(op)
                op.then_inc(w_ternary, 1)

            variances(0, 0)
            norm(0, 0)
            ternary(0, w1q)
            xt_lo(0, 0)
            dve.wait_ge(w_loaded[0], 16)
            split(wqk_raw, wqk)
            dve.wait_ge(w_loaded[2], 16)
            split(wv_raw, wv)
            ternary(1, w2q)

            def body(it, first, last):
                for u in range(2):
                    more = not (last and u == 1)
                    if more:
                        variances(it, u + 1)
                    for m in range(MT):
                        for f in range(2 * m, 2 * m + 2):
                            wait(dve, h_ready, it, 2 * FT, FT * u + f + 1)
                            nc.vector.tensor_tensor(hl[:, f, :], hf[:, f % 4, :], hh[:, f, :].bitcast(F32),
                                                    ALU.subtract).then_inc(hl_ready, 1)
                        wait(dve, qk_hi_ready, it, 2 * MT, MT * u + m + 1)
                        nc.vector.tensor_tensor(qk_st[:, m, 1, :], ps[:, 4 + m % 2, :],
                                                qk_st[:, m, 0, :].bitcast(F32),
                                                ALU.subtract).then_inc(qk_lo_ready, 1)
                        if m == 0 and more:
                            norm(it, u + 1)
                    if more:
                        xt_lo(it, u + 1)
                    wait(dve, xb_ready, it, 2, u + 1)
                    for t2 in range(TB // 2):
                        wait(dve, y_mm, it, TB, TB // 2 * u + t2 + 1)
                        for e in range(2):
                            yt = y_tile(it, u, 2 * t2 + e)
                            op = nc.vector.tensor_tensor(
                                yt, ps[:, t2, e * D:(e + 1) * D].rearrange("p (h c) -> p h c", h=DH), yt, ALU.add)
                        op.then_inc(y_ready, 1)

            looped(dve, B, {16, 2 * LN, 2, 2 * DH, 2 * FT, 2 * MT, TB}, body)

        @block.tensor
        def _(pe):
            def transposes(it, u):
                wait(pe, xn_ready, it, 2, u + 1)
                wait(pe, v_ready, it, 2 * TB, TB * (u - 1) + 2)
                for h in range(DH):
                    for t in range(TB):
                        mm = nc.tensor.transpose(ps[:, 6 + h, t * P:(t + 1) * P], xn[:, t, h * P:(h + 1) * P],
                                                 ident[:])
                    mm.then_inc(xt_mm, 1)

            def hidden(it, u, f):
                if f < 2:
                    wait(pe, h_ready, it, 2 * FT, FT * u - FT + f + 5)
                elif f < 4:
                    wait(pe, y_ready, it, TB, TB // 2 * u - TB // 2 + f - 1)
                else:
                    wait(pe, h_ready, it, 2 * FT, FT * u + f - 3)
                n = 0
                for part in range(2):
                    for h in range(DH):
                        mm = nc.tensor.matmul(ps[:, (f + 2) % 4, :], w1q[:, h, f * P:(f + 1) * P],
                                              xt[part][:, h, :], start=(n == 0), stop=(n == 3))
                        n += 1
                mm.then_inc(ffn1_mm, 1)

            def totals(n):
                pe.wait_ge(sums_ready, 2 * n + 2)
                nc.tensor.matmul(ps[:, 7, 2 * n:2 * n + 2], ones[:], part_sum[:, 2 * n:2 * n + 2],
                                 start=True, stop=True).then_inc(total_ready, 1)

            pe.wait_ge(ident_set, 2)
            pe.wait_ge(consts_set, 1)
            totals(0)
            pe.wait_ge(w_ternary, 1)
            transposes(0, 0)
            pe.wait_ge(xt_lo_ready, DH)
            totals(1)

            def body(it, first, last):
                for u in range(2):
                    wait(pe, xt_lo_ready, it, 2 * DH, DH * (u + 1))
                    for m in range(MT):
                        for f in range(2 * m, 2 * m + 2):
                            hidden(it, u, f)
                        if first and u == 0 and m == 0:
                            pe.wait_ge(w_split, 1)
                        if m < 2:
                            wait(pe, v_ready, it, 2 * TB, TB * u - TB + 3 + m)
                        else:
                            wait(pe, qk_lo_ready, it, 2 * MT, MT * u + m - 1)
                        n = 0
                        for a, c in ((0, 0), (1, 0), (0, 1)):
                            for h in range(DH):
                                mm = nc.tensor.matmul(ps[:, 4 + m % 2, :], wqk[a][:, h, m * P:(m + 1) * P],
                                                      xt[c][:, h, :], start=(n == 0), stop=(n == 5))
                                n += 1
                        mm.then_inc(qk_mm, 1)
                    if first and u == 0:
                        pe.wait_ge(w_split, 2)
                    for t in range(TB):
                        if t >= 2:
                            wait(pe, qk_lo_ready, it, 2 * MT, MT * u + t + 1)
                        n = 0
                        for a, c in ((0, 0), (0, 1), (1, 0)):
                            for h in range(DH):
                                mm = nc.tensor.matmul(ps[:, V_BANK[t], 0:D], xt[a][:, h, t * P:(t + 1) * P],
                                                      wv[c][:, h, :], start=(n == 0), stop=(n == 5))
                                n += 1
                        mm.then_inc(v_mm, 1)
                    if not (last and u == 1):
                        transposes(it, u + 1)
                    if first and u == 0:
                        pe.wait_ge(w_ternary, 2)
                    for t in range(TB):
                        if t % 2 == 0:
                            wait(pe, h_ready, it, 2 * FT, FT * (u + 1))
                            wait(pe, hl_ready, it, 2 * FT, FT * (u + 1))
                        n = 0
                        for hid in (hh, hl):
                            for f in range(FT):
                                mm = nc.tensor.matmul(ps[:, t // 2, t % 2 * D:(t % 2 + 1) * D],
                                                      hid[:, f, t * P:(t + 1) * P], w2q[:, f, :],
                                                      start=(n == 0), stop=(n == 2 * FT - 1))
                                n += 1
                        if t % 2:
                            mm.then_inc(y_mm, 1)

            looped(pe, B, {2, 2 * DH, 2 * FT, TB, 2 * TB, 2 * MT}, body)


def part_b(nc, qk_d, v_d, out, Y, ident):
    with ExitStack() as ctx:
        def sb(name, shape, dt=F32):
            return ctx.enter_context(nc.sbuf_tensor(name, shape, dt))

        def sem(name):
            return ctx.enter_context(nc.semaphore(name))

        sc = ctx.enter_context(nc.psum_tensor("ps_scores", [P, NS, BANK], F32))
        mx = ctx.enter_context(nc.psum_tensor("ps_maxima", [P, NS, BANK], F32))
        po = ctx.enter_context(nc.psum_tensor("ps_out", [P, BANK], F32))
        pt = ctx.enter_context(nc.psum_tensor("ps_turn", [P, BANK], F32))
        qs = sb("q_stack", [P, UN, 2, S], F32R)
        ks = sb("k_stack", [P, UN, 2, S], F32R)
        vt = sb("v_tile", [P, UN, NT, 2 * VC])
        pr = sb("probs", [P, NP, 4, BANK])
        mpart = sb("max_halves", [P, 2, SLOTS])
        mcol = sb("max_cols", [P, SLOTS // 2])
        mhi = sb("max_hi", [2 * NT, P], F32R)
        mlo = sb("max_lo", [2 * NT, P], F32R)
        osb = sb("o_t", [P, BANK])
        rec = sb("rec", [P, 2 * NT])
        on = sb("o_norm", [P, 2 * NT, HD])

        ones_set = sem("ones_set")
        zeros_set = sem("zeros_set")
        out_zeroed = sem("out_zeroed")
        loaded = [sem(f"loaded{r}") for r in range(UN)]
        scores_mm = sem("scores_mm")
        probs_ready = sem("probs_ready")
        max_mm = sem("max_mm")
        max_taken = sem("max_taken")
        cols_ready = sem("cols_ready")
        cols_turned = sem("cols_turned")
        row_hi_ready = sem("row_hi_ready")
        row_lo_ready = sem("row_lo_ready")
        rows_placed = [sem("rows_placed0"), sem("rows_placed1")]
        pv_mm = sem("pv_mm")
        o_copied = sem("o_copied")
        o_turned = sem("o_turned")
        rec_ready = sem("rec_ready")
        o_normed = sem("o_normed")
        y_added = sem("y_added")
        y_stored = sem("y_stored")

        def waitp(eng, s, it, j, per, add):
            wait(eng, s, it, UN * per, per * j + add)

        def bank(j, s):
            return (j % UN * SLOTS + s) % NS

        def ring_user(j, s):
            k = j % UN * SLOTS + s
            last = k - NS if k >= NS else k + (UN * SLOTS - 1 - k) // NS * NS - UN * SLOTS
            return last + 1 - j % UN * SLOTS

        def lead(t):
            return (1, t + LEAD) if t + LEAD < STEPS else (2, t + LEAD - STEPS)

        TURN = STEPS - LEAD

        block = ctx.enter_context(nc.Block())

        @block.sync
        def _(sp):
            def load(pair, r):
                for a in range(2):
                    for qk, st in ((0, qs), (1, ks)):
                        two = qk_d[qk, bass.ds(2 * pair + a, 1)][0]
                        src = two[0].unsqueeze(0).broadcast_to([2, HD, S]) if qk == 0 else two
                        sp.dma_start(st[0:2 * HD, r, a, :].bitcast(F32), src).then_inc(loaded[r], 16)
                        sp.dma_start(st[2 * HD:QROWS, r, a, :].bitcast(F32),
                                     two[1 - qk]).then_inc(loaded[r], 16)
                sp.dma_start(vt[:, r], v_d[bass.ds(pair, 1)][0]).then_inc(loaded[r], 16)

            def place(it, j, r, parity):
                waitp(sp, row_lo_ready, it, j, 1, 1)
                for a in range(2):
                    for n, part in enumerate((mhi, mlo)):
                        row = MROW + n
                        sp.dma_start(qs[row:row + 1, r, a, :].bitcast(F32),
                                     part[a * NT:(a + 1) * NT, :].bitcast(F32)).then_inc(rows_placed[parity], 16)

            for r in range(UN - 1):
                sp.wait_ge(ones_set, r + 1)
                sp.wait_ge(zeros_set, r + 1)
                load(r, r)
            place(0, 0, 0, 0)
            sp.wait_ge(ones_set, UN)
            sp.wait_ge(zeros_set, UN)

            def body(it, first, last):
                for j in range(UN):
                    if not (last and j > 0):
                        pair = UN * at(it) + j + 3
                        if not isinstance(it, int):
                            pair = sp.snap(pair)
                        wait_all(sp, (scores_mm, it, UN * SLOTS, SLOTS * j), (pv_mm, it, UN * STEPS, STEPS * j))
                        load(pair, (j + 3) % UN)
                    if not (last and j == UN - 1):
                        place(it, j + 1, (j + 1) % UN, (j + 1) % 2)

            looped(sp, NIT, {UN, UN * SLOTS, UN * STEPS}, body)

        @block.gpsimd
        def _(pool):
            for r in range(UN):
                nc.gpsimd.memset(ks[:, r].bitcast(F32), 1.0).then_inc(ones_set, 1)

            def body(b, first, last):
                for g in range(2):
                    for j in range(UN):
                        wait(pool, o_normed, b, 2 * UN, UN * g + j + 1)
                        yv = Y[:, bass.ds(2 * at(b) + g, 1), :, j * 2 * HD:(j + 1) * 2 * HD].rearrange(
                            "p o (q t) c -> p t (o q) c", q=2)
                        nc.gpsimd.tensor_tensor(yv, yv, on[:].rearrange("p (t q a) c -> p t q (a c)", q=2, a=2),
                                                ALU.add).then_inc(y_added, 1)
                    wait(pool, y_added, b, 2 * UN, UN * (g + 1))
                    pool.dma_start(out[bass.ds(at(b), 1), :, g * P:(g + 1) * P].rearrange(
                        "o (t p) c -> p (o t) c", p=P), Y[:, bass.ds(2 * at(b) + g, 1)].rearrange(
                        "p o t c -> p (o t) c")).then_inc(y_stored, 16)

            looped(pool, B, {2 * UN}, body)
            pool.wait_ge(y_stored, 16 * NIT)

        @block.scalar
        def _(act):
            def exps(it, j, t, slots):
                for s in slots:
                    waitp(act, scores_mm, it, j, SLOTS, 4 * t + s + 1)
                    if s == 0:
                        waitp(act, pv_mm, it, j, STEPS, t - NP + 1)
                    nc.scalar.activation(pr[:, t % NP, s, :], sc[:, bank(j, 4 * t + s), :], ACT.Exp,
                                         scale=1.0 / D ** 0.5).then_inc(probs_ready, 1)

            def row_hi(it, j):
                waitp(act, cols_turned, it, j, 1, 1)
                waitp(act, row_lo_ready, it, j, 1, 0)
                wait(act, rows_placed[(j - 1) % 2], it, 32 * UN, 64 * ((j - 1) // 2 + 1))
                nc.scalar.activation(mhi[:], pt[0:2 * NT, 0:P], ACT.Copy, scale=-1.0).then_inc(row_hi_ready, 1)

            def copy_o(it, j):
                waitp(act, pv_mm, it, j, STEPS, STEPS)
                waitp(act, o_turned, it, j, 1, 0)
                nc.scalar.activation(osb[:], po[:], ACT.Copy).then_inc(o_copied, 1)

            row_hi(0, 0)

            def body(it, first, last):
                for j in range(UN):
                    for t in range(STEPS):
                        exps(it, j, t, (0, 1))
                        if t == 0 and not (first and j == 0):
                            copy_o(it, j - 1)
                        exps(it, j, t, (2, 3))
                        if t == TURN and not (last and j == UN - 1):
                            row_hi(it, j + 1)

            looped(act, NIT, {UN, UN * SLOTS, UN * STEPS, 32 * UN}, body)
            copy_o(NIT - 1, UN - 1)

        @block.vector
        def _(dve):
            nc.vector.memset(po[:], 0.0).then_inc(out_zeroed, 1)
            for r in range(UN):
                nc.vector.memset(qs[:, r].bitcast(F32), 0.0).then_inc(zeros_set, 1)

            def maxima(it, j, g):
                for s in range(4 * g, 4 * g + 4):
                    waitp(dve, max_mm, it, j, SLOTS, s + 1)
                    nc.vector.tensor_reduce(mpart[:, j % 2, s:s + 1], mx[:, bank(j, s), :], AX_X,
                                            ALU.max).then_inc(max_taken, 1)
                if g == STEPS - 1:
                    waitp(dve, max_taken, it, j, SLOTS, SLOTS)
                    waitp(dve, cols_turned, it, j, 1, 0)
                    nc.vector.tensor_reduce(mcol[:], mpart[:, j % 2, :].rearrange("p (n k) -> p n k", k=2), AX_X,
                                            ALU.max).then_inc(cols_ready, 1)

            def row_lo(it, j):
                waitp(dve, row_hi_ready, it, j, 1, 1)
                nc.vector.scalar_tensor_tensor(mlo[:], pt[0:2 * NT, 0:P], -1.0, mhi[:].bitcast(F32), ALU.mult,
                                               ALU.subtract).then_inc(row_lo_ready, 1)

            def norm_o(it, j):
                waitp(dve, o_turned, it, j, 1, 1)
                turned = pt[:].rearrange("p (n c) -> p n c", c=32)
                nc.vector.reciprocal(rec[:], turned[:, :, HD]).then_inc(rec_ready, 1)
                waitp(dve, rec_ready, it, j, 1, 1)
                waitp(dve, y_added, it, j, 1, 0)
                nc.vector.tensor_tensor(on[:], turned[:, :, 0:HD],
                                        rec[:].unsqueeze(2).broadcast_to([P, 2 * NT, HD]),
                                        ALU.mult).then_inc(o_normed, 1)

            for g in range(STEPS):
                maxima(0, 0, g)
            row_lo(0, 0)
            for g in range(LEAD):
                maxima(0, 1, g)

            def body(it, first, last):
                for j in range(UN):
                    for t in range(STEPS):
                        if t == 2 and not (first and j == 0):
                            norm_o(it, j - 1)
                        ahead, g = lead(t)
                        if not (last and j + ahead >= UN):
                            maxima(it, j + ahead, g)
                        if t == TURN and not (last and j == UN - 1):
                            row_lo(it, j + 1)

            looped(dve, NIT, {UN, UN * SLOTS}, body)
            norm_o(NIT - 1, UN - 1)

        @block.tensor
        def _(pe):
            def max_slot(it, j, s):
                r = j % UN
                a, qt, kh = s // (2 * NT), s // 2 % NT, s % 2
                if s == 0:
                    wait(pe, loaded[r], it, 9 * 16, 9 * 16 * (j // UN + 1))
                waitp(pe, max_taken, it, j, SLOTS, ring_user(j, s))
                nc.tensor.matmul(mx[:, bank(j, s), :], qs[0:MROW, r, a, qt * P:(qt + 1) * P],
                                 ks[0:MROW, r, a, kh * BANK:(kh + 1) * BANK],
                                 start=True, stop=True).then_inc(max_mm, 1)

            def score_slot(it, j, s):
                r = j % UN
                kt, a, qh = s // 4, s // 2 % 2, s % 2
                if s == 0:
                    wait(pe, rows_placed[j % 2], it, 32 * UN, 64 * (j // 2 + 1))
                waitp(pe, probs_ready, it, j, SLOTS, ring_user(j, s))
                nc.tensor.matmul(sc[:, bank(j, s), :], ks[0:CR, r, a, kt * P:(kt + 1) * P],
                                 qs[0:CR, r, a, qh * BANK:(qh + 1) * BANK],
                                 start=True, stop=True).then_inc(scores_mm, 1)

            def products(it, j, t):
                r = j % UN
                waitp(pe, probs_ready, it, j, SLOTS, 4 * t + 4)
                if t == 0:
                    waitp(pe, o_copied, it, j, 1, 0)
                for g in range(4):
                    qh, a = g // 2, g % 2
                    mm = nc.tensor.matmul(po[32 * g:32 * g + VC, :], vt[:, r, t, a * VC:(a + 1) * VC],
                                          pr[:, t % NP, 2 * a + qh, :], start=(t == 0),
                                          stop=(t == STEPS - 1))
                mm.then_inc(pv_mm, 1)

            def turn_cols(it, j):
                waitp(pe, cols_ready, it, j, 1, 1)
                waitp(pe, o_normed, it, j, 1, -1)
                nc.tensor.transpose(pt[0:2 * NT, 0:P], mcol[:], ident[:]).then_inc(cols_turned, 1)

            def turn_o(it, j, final=False):
                waitp(pe, o_copied, it, j, 1, 1)
                if final:
                    waitp(pe, o_normed, it, j, 1, 0)
                else:
                    waitp(pe, row_lo_ready, it, j, 1, 2)
                for n in range(4):
                    mm = nc.tensor.transpose(pt[:, n * P:(n + 1) * P], osb[:, n * P:(n + 1) * P], ident[:])
                mm.then_inc(o_turned, 1)

            pe.wait_ge(out_zeroed, 1)
            for s in range(SLOTS):
                max_slot(0, 0, s)
            for s in range(4 * LEAD):
                max_slot(0, 1, s)
                if s == 1:
                    turn_cols(0, 0)

            def body(it, first, last):
                for j in range(UN):
                    for t in range(STEPS):
                        ahead, g = lead(t)
                        maxing = not (last and j + ahead >= UN)
                        for n in range(4):
                            score_slot(it, j, 4 * t + n)
                            if maxing:
                                max_slot(it, j + ahead, 4 * g + n)
                            if n == 2 and t == TURN and not (last and j == UN - 1):
                                turn_cols(it, j + 1)
                            if n == 1:
                                if t:
                                    products(it, j, t - 1)
                                elif not (first and j == 0):
                                    products(it, j - 1, STEPS - 1)
                        if t == 1 and not (first and j == 0):
                            turn_o(it, j - 1)

            looped(pe, NIT, {UN, UN * SLOTS, 9 * 16, 32 * UN}, body)
            products(NIT - 1, UN - 1, STEPS - 1)
            turn_o(NIT - 1, UN - 1, final=True)


def program(nc, x, wqkt, wvt, w1t, w2t, b1t, b2, out):
    qk_d = nc.dram_tensor("qk_parts", [2, B * H, 2, HD, S], F32, kind="Internal").ap()
    v_d = nc.dram_tensor("v_pairs", [PAIRS, P, NT, 2 * VC], F32, kind="Internal").ap()
    with ExitStack() as ctx:
        Y = ctx.enter_context(nc.sbuf_tensor("Y", [P, DH * B, NT, P], F32))
        ident = ctx.enter_context(nc.sbuf_tensor("ident", [P, P], F32))
        part_a(nc, x, wqkt, wvt, w1t, w2t, b1t, b2, qk_d, v_d, Y, ident)
        part_b(nc, qk_d, v_d, out, Y, ident)


def kernel(**inputs):
    import numpy as np
    import concourse.bacc as bacc
    from concourse.bass_utils import run_bass_kernel_spmd

    w = {n: np.asarray(inputs[f"L0_{n}"]) for n in ("attn_Wq", "attn_Wk", "attn_Wv", "ffn_W1", "ffn_W2",
                                                    "ffn_b1", "ffn_b2")}
    arrays = {
        "x": np.asarray(inputs["L0_attn_x"]),
        "wqkt": np.concatenate([w["attn_Wq"].T, w["attn_Wk"].T], axis=1),
        "wvt": w["attn_Wv"].T,
        "w1t": w["ffn_W1"].T,
        "w2t": w["ffn_W2"].T,
        "b1t": w["ffn_b1"].reshape(FT, P).T,
        "b2": w["ffn_b2"],
    }
    arrays = {n: np.ascontiguousarray(a) for n, a in arrays.items()}
    nc = bacc.Bacc("TRN2", target_bir_lowering=False, num_devices=1)
    args = [nc.dram_tensor(n, a.shape, F32, kind="ExternalInput").ap() for n, a in arrays.items()]
    out = nc.dram_tensor("out", (B, S, D), F32, kind="ExternalOutput").ap()
    program(nc, *args, out)
    r = run_bass_kernel_spmd(nc, [arrays], core_ids=[0])
    return r.results[0]["out"]
```

```python
import itertools
from contextlib import ExitStack

import concourse.bass as bass
from concourse import mybir

F32 = mybir.dt.float32
F32R = mybir.dt.float32r
ALU = mybir.AluOpType
ACT = mybir.ActivationFunctionType
AX_X = mybir.AxisListType.X

P = 128
BANK = 512
EPS = 1e-05

B, S, D = 8, 1024, 256
H, HD = 16, 16
FF = 4 * D
DH = D // P
FT = FF // P
BLK = 512
TB = BLK // P
NT = S // P
MT = 2 * D // P
PAIRS = B * H // 2
VC = HD + 1
UN = 4
NIT = PAIRS // UN
LN = 9
V_BANK = (6, 7, 4, 5)
LEAD = 4
STEPS = NT
SLOTS = 4 * STEPS
NS = 3
SCORE_START = 26
MAX_START = 10
NP = 4
LOADS = 9 * 16
QROWS = 3 * HD
MROW = 96
CR = MROW + 2


REGISTERS = itertools.count()


def register(eng):
    return eng.alloc_register(f"count{next(REGISTERS)}")


class Turn:

    def __init__(self, eng, it, multiples):
        self.at = it
        self.times = {}
        for m in sorted(multiples):
            self.times[m] = register(eng)
            eng.reg_mul(self.times[m], eng.to_reg(it), m)


def at(it):
    return it if isinstance(it, int) else it.at


def wait_all(eng, *waits):
    values = []
    for sem, it, per, add in waits:
        if not isinstance(it, int):
            value = it.times[per]
            if add:
                value = register(eng)
                eng.reg_add(value, it.times[per], add)
            values.append((sem, value))
        elif per * it + add > 0:
            values.append((sem, per * it + add))
    for sem, value in values:
        eng.wait_ge(sem, value)


def wait(eng, sem, it, per, add):
    wait_all(eng, (sem, it, per, add))


def looped(eng, n, multiples, body):
    body(0, True, False)
    with eng.Fori(1, n - 1) as it:
        body(Turn(eng, it, multiples), False, False)
    body(n - 1, False, True)


def part_a(nc, x, wqkt, wvt, w1t, w2t, b1t, b2, qk_d, v_d, Y, ident):
    with ExitStack() as ctx:
        def sb(name, shape, dt=F32):
            return ctx.enter_context(nc.sbuf_tensor(name, shape, dt))

        def sem(name):
            return ctx.enter_context(nc.semaphore(name))

        ps = ctx.enter_context(nc.psum_tensor("psA", [P, 8, BANK], F32))
        wqk_raw = sb("wqk_raw", [P, DH, 2 * D])
        wv_raw = sb("wv_raw", [P, DH, D])
        wf_raw = [sb("w1_raw", [P, DH, FF]), sb("w2_raw", [P, FT, D])]
        mag = sb("mag", [P, 1024])
        part_sum = sb("part_sum", [P, 4])
        thresh = sb("thresh", [P, 4])
        ones = sb("ones", [P, P])
        wqk = [sb("wqk_hi", [P, DH, 2 * D], F32R), sb("wqk_lo", [P, DH, 2 * D], F32R)]
        wv = [sb("wv_hi", [P, DH, D], F32R), sb("wv_lo", [P, DH, D], F32R)]
        w1q = sb("w1q", [P, DH, FF], F32R)
        w2q = sb("w2q", [P, FT, D], F32R)
        b1c = sb("b1c", [P, FT])
        b2b = sb("b2b", [P, D])
        xin = sb("xin", [P, 2, TB, D])
        xn = sb("xn", [P, TB, D])
        stats = sb("stats", [P, TB, 6])
        pair = sb("pair", [P, TB, 2])
        diff = sb("diff", [P, TB])
        mean = sb("mean", [P, TB])
        var = sb("var", [P, TB])
        root = sb("root", [P, TB])
        tmp = sb("tmp", [P, TB])
        rstd = sb("rstd", [P, TB])
        xt = [sb("xt_hi", [P, DH, BLK], F32R), sb("xt_lo", [P, DH, BLK], F32R)]
        qk_st = sb("qk_st", [P, MT, 2, BLK], F32R)
        v_st = sb("v_st", [P, 2, H // 2, TB, 2 * VC])
        hf = sb("hf", [P, 4, BLK])
        hh = sb("hh", [P, FT, BLK], F32R)
        hl = sb("hl", [P, FT, BLK], F32R)

        qk_a = qk_d.rearrange("s (b m h) r d t -> s b m h r d t", b=B, m=DH)
        v_a = v_d.rearrange("(b a) p t c -> b a p t c", b=B)

        wqk_loaded = sem("wqk_loaded")
        wv_loaded = sem("wv_loaded")
        wf_loaded = [sem("w1_loaded"), sem("w2_loaded")]
        b1_loaded = sem("b1_loaded")
        b2_loaded = sem("b2_loaded")
        x_loaded = [sem("x_loaded0"), sem("x_loaded1")]
        consts_set = sem("consts_set")
        ident_set = sem("ident_set")
        dve_chain = sem("dve_chain")
        sums_ready = sem("sums_ready")
        total_ready = sem("total_ready")
        thresh_ready = sem("thresh_ready")
        w_split = sem("w_split")
        w_ternary = sem("w_ternary")
        ln_step = sem("ln_step")
        var_ready = sem("var_ready")
        root_ready = sem("root_ready")
        xn_ready = sem("xn_ready")
        xt_mm = sem("xt_mm")
        xt_hi_ready = sem("xt_hi_ready")
        xt_lo_ready = sem("xt_lo_ready")
        ffn1_mm = sem("ffn1_mm")
        h_ready = sem("h_ready")
        hl_ready = sem("hl_ready")
        qk_mm = sem("qk_mm")
        qk_hi_ready = sem("qk_hi_ready")
        qk_lo_ready = sem("qk_lo_ready")
        v_mm = sem("v_mm")
        v_ready = sem("v_ready")
        xb_ready = sem("xb_ready")
        y_mm = sem("y_mm")
        y_ready = sem("y_ready")
        qk_stored = [sem(f"qk_stored{m}") for m in range(MT)]
        v_stored = [sem("v_stored0"), sem("v_stored1")]

        def y_tile(it, u, t):
            yt = Y[:, bass.ds(2 * at(it), 2), u * TB + t, :]
            return yt

        block = ctx.enter_context(nc.Block())

        @block.sync
        def _(sp):
            def load_x(b, u):
                src = x[bass.ds(b, 1), u * BLK:(u + 1) * BLK, :].rearrange("o (t p) d -> p (o t) d", p=P)
                sp.dma_start(xin[:, u, :, :], src).then_inc(x_loaded[u], 16)

            load_x(0, 0)
            sp.dma_start(wf_raw[0][:], w1t.rearrange("(h p) n -> p h n", p=P)).then_inc(wf_loaded[0], 16)
            sp.dma_start(wqk_raw[:], wqkt.rearrange("(h p) n -> p h n", p=P)).then_inc(wqk_loaded, 16)
            sp.dma_start(wf_raw[1][:], w2t.rearrange("(t p) n -> p t n", p=P)).then_inc(wf_loaded[1], 16)
            sp.dma_start(wv_raw[:], wvt.rearrange("(h p) n -> p h n", p=P)).then_inc(wv_loaded, 16)
            sp.dma_start(b1c[:], b1t).then_inc(b1_loaded, 16)
            sp.dma_start(b2b[:], b2.partition_broadcast(P)).then_inc(b2_loaded, 16)
            load_x(0, 1)

            def body(it, first, last):
                for u in range(2):
                    for m in range(MT):
                        wait(sp, qk_lo_ready, it, 2 * MT, MT * u + m + 1)
                        heads = P // HD
                        for part in range(2):
                            dst = qk_a[m // DH, bass.ds(at(it), 1), m % DH, :, part, :, u * BLK:(u + 1) * BLK]
                            sp.dma_start(dst.rearrange("o h d t -> (o h) d t"),
                                         qk_st[:, m, part, :].bitcast(F32)).then_inc(qk_stored[m], 16)
                    wait(sp, v_ready, it, 2 * TB, TB * u + TB)
                    sp.dma_start(v_a[bass.ds(at(it), 1), :, :, u * TB:(u + 1) * TB, :].rearrange(
                        "o a p t c -> p (o a) t c"), v_st[:, u]).then_inc(v_stored[u], 16)
                    if not last:
                        wait_all(sp, (xn_ready, it, 2, u + 1), (xb_ready, it, 2, u + 1))
                        load_x(at(it) + 1, u)

            looped(sp, B, {2 * MT, 2 * TB, 2}, body)
            for m in range(MT):
                sp.wait_ge(qk_stored[m], 2 * B * 32)
            for u in range(2):
                sp.wait_ge(v_stored[u], B * 16)

        @block.gpsimd
        def _(pool):
            nc.gpsimd.memset(ident[:], 0.0).then_inc(ident_set, 1)
            nc.gpsimd.memset(ones[:], 1.0).then_inc(consts_set, 1)
            pool.wait_ge(ident_set, 1)
            nc.gpsimd.affine_select(out=ident[:], in_=ident[:], compare_op=ALU.not_equal, fill=1.0, base=0,
                                    pattern=[[-1, P]], channel_multiplier=1).then_inc(ident_set, 1)
            nc.gpsimd.memset(v_st[:], 1.0).then_inc(consts_set, 1)
            pool.wait_ge(b2_loaded, 16)

            def body(it, first, last):
                for u in range(2):
                    wait(pool, x_loaded[u], it, 16, 16)
                    for t in range(TB):
                        op = nc.gpsimd.tensor_tensor(y_tile(it, u, t),
                                                     xin[:, u, t, :].rearrange("p (h c) -> p h c", h=DH),
                                                     b2b[:].rearrange("p (h c) -> p h c", h=DH), ALU.add)
                    op.then_inc(xb_ready, 1)

            looped(pool, B, {16}, body)

        @block.scalar
        def _(act):
            act.wait_ge(var_ready, 1)
            nc.scalar.activation(root[:], var[:], ACT.Sqrt).then_inc(root_ready, 1)

            def sums(n):
                act.wait_ge(wf_loaded[n], 16)
                flat = wf_raw[n][:].rearrange("p a n -> p (a n)")
                for h in range(2):
                    nc.scalar.activation(hf[:, 0:2, :].rearrange("p a n -> p (a n)"),
                                         flat[:, h * 1024:(h + 1) * 1024], ACT.Abs,
                                         accum_out=part_sum[:, 2 * n + h:2 * n + h + 1]).then_inc(sums_ready, 1)
                    act.wait_ge(sums_ready, 2 * n + h + 1)

            def xt_hi(it, u):
                for h in range(DH):
                    wait(act, xt_mm, it, 2 * DH, DH * u + h + 1)
                    nc.scalar.activation(xt[0][:, h, :], ps[:, 6 + h, :], ACT.Copy).then_inc(xt_hi_ready, 1)

            sums(0)
            xt_hi(0, 0)
            sums(1)
            act.wait_ge(b1_loaded, 16)
            act.wait_ge(consts_set, 2)

            def body(it, first, last):
                for u in range(2):
                    more = not (last and u == 1)
                    for m in range(MT):
                        for f in range(2 * m, 2 * m + 2):
                            wait(act, ffn1_mm, it, 2 * FT, FT * u + f + 1)
                            wait(act, hl_ready, it, 2 * FT, FT * u + f - 3)
                            bank = ps[:, (f + 2) % 4, :]
                            nc.scalar.activation(hf[:, f % 4, :], bank, ACT.Relu, bias=b1c[:, f:f + 1])
                            nc.scalar.activation(hh[:, f, :], bank, ACT.Relu,
                                                 bias=b1c[:, f:f + 1]).then_inc(h_ready, 1)
                        wait(act, qk_mm, it, 2 * MT, MT * u + m + 1)
                        wait(act, qk_stored[m], it, 64, 32 * u)
                        nc.scalar.activation(qk_st[:, m, 0, :], ps[:, 4 + m % 2, :],
                                             ACT.Copy).then_inc(qk_hi_ready, 1)
                        if m == 0 and more:
                            wait(act, var_ready, it, 2, u + 2)
                            nc.scalar.activation(root[:], var[:], ACT.Sqrt).then_inc(root_ready, 1)
                    for t in range(TB):
                        wait(act, v_mm, it, 2 * TB, TB * u + t + 1)
                        if t == 0:
                            wait(act, v_stored[u], it, 16, 0)
                        nc.scalar.activation(
                            v_st[:, u, :, t, :].rearrange("p a (e c) -> p a e c", e=2)[:, :, :, 0:HD],
                            ps[:, V_BANK[t], 0:D].rearrange("p (a e c) -> p a e c", e=2, c=HD),
                            ACT.Copy).then_inc(v_ready, 1)
                    if more:
                        xt_hi(it, u + 1)

            looped(act, B, {2 * DH, 2 * FT, 2, 2 * MT, 64, 2 * TB, 16}, body)

        @block.vector
        def _(dve):
            chained = [0]

            def link(ins):
                chained[0] += 1
                ins.then_inc(dve_chain, 1)
                dve.wait_ge(dve_chain, chained[0])

            def variances(it, u):
                wait(dve, x_loaded[u % 2], it, 16, 16 * (u // 2) + 16)
                for t in range(TB):
                    op = nc.vector.bn_stats(stats[:, t, :], xin[:, u % 2, t, :])
                op.then_inc(ln_step, 1)
                wait(dve, ln_step, it, 2 * LN, LN * u + 1)
                nc.vector.tensor_tensor(diff[:], stats[:, :, 1], stats[:, :, 4], ALU.subtract)
                nc.vector.tensor_tensor(pair[:], stats[:, :, 1:3], stats[:, :, 4:6],
                                        ALU.add).then_inc(ln_step, 1)
                wait(dve, ln_step, it, 2 * LN, LN * u + 2)
                nc.vector.tensor_tensor(diff[:], diff[:], diff[:], ALU.mult)
                nc.vector.tensor_scalar(mean[:], pair[:, :, 0], 0.5, None, ALU.mult).then_inc(ln_step, 1)
                wait(dve, ln_step, it, 2 * LN, LN * u + 3)
                nc.vector.tensor_scalar(diff[:], diff[:], 0.25, EPS, ALU.mult, ALU.add).then_inc(ln_step, 1)
                wait(dve, ln_step, it, 2 * LN, LN * u + 4)
                nc.vector.scalar_tensor_tensor(var[:], pair[:, :, 1], 1.0 / D, diff[:], ALU.mult,
                                               ALU.add).then_inc(var_ready, 1)

            def norm(it, u):
                wait(dve, root_ready, it, 2, u + 1)
                nc.vector.reciprocal(tmp[:], root[:]).then_inc(ln_step, 1)
                wait(dve, ln_step, it, 2 * LN, LN * u + 5)
                nc.vector.tensor_tensor(tmp[:], var[:], tmp[:], ALU.mult).then_inc(ln_step, 1)
                wait(dve, ln_step, it, 2 * LN, LN * u + 6)
                nc.vector.scalar_tensor_tensor(tmp[:], root[:], 1.0, tmp[:], ALU.mult,
                                               ALU.add).then_inc(ln_step, 1)
                wait(dve, ln_step, it, 2 * LN, LN * u + 7)
                nc.vector.reciprocal(rstd[:], tmp[:]).then_inc(ln_step, 1)
                wait(dve, ln_step, it, 2 * LN, LN * u + 8)
                nc.vector.tensor_scalar(rstd[:], rstd[:], 2.0, None, ALU.mult).then_inc(ln_step, 1)
                wait(dve, ln_step, it, 2 * LN, LN * u + 9)
                wait(dve, xt_mm, it, 2 * DH, DH * u)
                for t in range(TB):
                    op = nc.vector.tensor_scalar(xn[:, t, :], xin[:, u % 2, t, :], mean[:, t:t + 1],
                                                 rstd[:, t:t + 1], ALU.subtract, ALU.mult)
                op.then_inc(xn_ready, 1)

            def xt_lo(it, u):
                for h in range(DH):
                    wait(dve, xt_hi_ready, it, 2 * DH, DH * u + h + 1)
                    nc.vector.tensor_tensor(xt[1][:, h, :], ps[:, 6 + h, :], xt[0][:, h, :].bitcast(F32),
                                            ALU.subtract).then_inc(xt_lo_ready, 1)

            def split(raw, parts):
                link(nc.vector.tensor_copy(parts[0][:], raw[:]))
                nc.vector.tensor_tensor(parts[1][:], raw[:], parts[0][:].bitcast(F32),
                                        ALU.subtract).then_inc(w_split, 1)

            def threshold(n):
                dve.wait_ge(total_ready, n + 1)
                c = 2 * n
                link(nc.vector.tensor_reduce(thresh[:, c:c + 1], ps[:, 4 + n, 0:2], AX_X, ALU.add))
                link(nc.vector.tensor_scalar(thresh[:, c:c + 1], thresh[:, c:c + 1], 1.0 / (FF * D), EPS,
                                             ALU.mult, ALU.add))
                link(nc.vector.tensor_scalar(thresh[:, c + 1:c + 2], thresh[:, c:c + 1], -0.5, None, ALU.mult))
                nc.vector.tensor_scalar(thresh[:, c:c + 1], thresh[:, c:c + 1], 0.5, None,
                                        ALU.mult).then_inc(thresh_ready, 1)
                dve.wait_ge(thresh_ready, n + 1)

            def ternary(n, out):
                c = 2 * n
                raw = wf_raw[n][:].rearrange("p a n -> p (a n)")
                flat = out[:].rearrange("p a n -> p (a n)")
                for h in range(2):
                    half = raw[:, h * 1024:(h + 1) * 1024]
                    link(nc.vector.tensor_scalar(mag[:], half, thresh[:, c + 1:c + 2], None, ALU.is_lt))
                    op = nc.vector.scalar_tensor_tensor(flat[:, h * 1024:(h + 1) * 1024], half,
                                                        thresh[:, c:c + 1], mag[:], ALU.is_gt, ALU.subtract)
                    if h == 0:
                        link(op)
                op.then_inc(w_ternary, 1)

            variances(0, 0)
            norm(0, 0)
            threshold(0)
            ternary(0, w1q)
            xt_lo(0, 0)
            dve.wait_ge(wqk_loaded, 16)
            split(wqk_raw, wqk)
            threshold(1)

            def body(it, first, last):
                for u in range(2):
                    more = not (last and u == 1)
                    if more:
                        variances(it, u + 1)
                    for m in range(MT):
                        for f in range(2 * m, 2 * m + 2):
                            wait(dve, h_ready, it, 2 * FT, FT * u + f + 1)
                            nc.vector.tensor_tensor(hl[:, f, :], hf[:, f % 4, :], hh[:, f, :].bitcast(F32),
                                                    ALU.subtract).then_inc(hl_ready, 1)
                        wait(dve, qk_hi_ready, it, 2 * MT, MT * u + m + 1)
                        nc.vector.tensor_tensor(qk_st[:, m, 1, :], ps[:, 4 + m % 2, :],
                                                qk_st[:, m, 0, :].bitcast(F32),
                                                ALU.subtract).then_inc(qk_lo_ready, 1)
                        if m == 0 and more:
                            norm(it, u + 1)
                        if first and u == 0 and m == 0:
                            dve.wait_ge(wv_loaded, 16)
                            split(wv_raw, wv)
                        if first and u == 0 and m == 2:
                            dve.wait_ge(w_ternary, 1)
                            ternary(1, w2q)
                    if more:
                        xt_lo(it, u + 1)
                    wait(dve, xb_ready, it, 2, u + 1)
                    for t2 in range(TB // 2):
                        wait(dve, y_mm, it, TB, TB // 2 * u + t2 + 1)
                        for e in range(2):
                            yt = y_tile(it, u, 2 * t2 + e)
                            op = nc.vector.tensor_tensor(
                                yt, ps[:, t2, e * D:(e + 1) * D].rearrange("p (h c) -> p h c", h=DH), yt, ALU.add)
                        op.then_inc(y_ready, 1)

            looped(dve, B, {16, 2 * LN, 2, 2 * DH, 2 * FT, 2 * MT, TB}, body)

        @block.tensor
        def _(pe):
            def transposes(it, u):
                wait(pe, xn_ready, it, 2, u + 1)
                wait(pe, v_ready, it, 2 * TB, TB * (u - 1) + 2)
                for h in range(DH):
                    for t in range(TB):
                        mm = nc.tensor.transpose(ps[:, 6 + h, t * P:(t + 1) * P], xn[:, t, h * P:(h + 1) * P],
                                                 ident[:])
                    mm.then_inc(xt_mm, 1)

            def hidden(it, u, f):
                if f < 2:
                    wait(pe, h_ready, it, 2 * FT, FT * u - FT + f + 5)
                elif f < 4:
                    wait(pe, y_ready, it, TB, TB // 2 * u - TB // 2 + f - 1)
                else:
                    wait(pe, h_ready, it, 2 * FT, FT * u + f - 3)
                n = 0
                for part in range(2):
                    for h in range(DH):
                        mm = nc.tensor.matmul(ps[:, (f + 2) % 4, :], w1q[:, h, f * P:(f + 1) * P],
                                              xt[part][:, h, :], start=(n == 0), stop=(n == 3))
                        n += 1
                mm.then_inc(ffn1_mm, 1)

            def totals(n):
                pe.wait_ge(sums_ready, 2 * n + 2)
                nc.tensor.matmul(ps[:, 4 + n, 0:2], ones[:], part_sum[:, 2 * n:2 * n + 2],
                                 start=True, stop=True).then_inc(total_ready, 1)

            pe.wait_ge(ident_set, 2)
            pe.wait_ge(consts_set, 1)
            totals(0)
            transposes(0, 0)
            totals(1)
            pe.wait_ge(w_ternary, 1)

            def body(it, first, last):
                for u in range(2):
                    wait(pe, xt_lo_ready, it, 2 * DH, DH * (u + 1))
                    for m in range(MT):
                        for f in range(2 * m, 2 * m + 2):
                            hidden(it, u, f)
                        if first and u == 0 and m == 0:
                            pe.wait_ge(w_split, 1)
                        if first and u == 0 and m == 1:
                            pe.wait_ge(thresh_ready, 2)
                        if m < 2:
                            wait(pe, v_ready, it, 2 * TB, TB * u - TB + 3 + m)
                        else:
                            wait(pe, qk_lo_ready, it, 2 * MT, MT * u + m - 1)
                        n = 0
                        for a, c in ((0, 0), (1, 0), (0, 1)):
                            for h in range(DH):
                                mm = nc.tensor.matmul(ps[:, 4 + m % 2, :], wqk[a][:, h, m * P:(m + 1) * P],
                                                      xt[c][:, h, :], start=(n == 0), stop=(n == 5))
                                n += 1
                        mm.then_inc(qk_mm, 1)
                    if first and u == 0:
                        pe.wait_ge(w_split, 2)
                    for t in range(TB):
                        if t >= 2:
                            wait(pe, qk_lo_ready, it, 2 * MT, MT * u + t + 1)
                        n = 0
                        for a, c in ((0, 0), (0, 1), (1, 0)):
                            for h in range(DH):
                                mm = nc.tensor.matmul(ps[:, V_BANK[t], 0:D], xt[a][:, h, t * P:(t + 1) * P],
                                                      wv[c][:, h, :], start=(n == 0), stop=(n == 5))
                                n += 1
                        mm.then_inc(v_mm, 1)
                    if not (last and u == 1):
                        transposes(it, u + 1)
                    if first and u == 0:
                        pe.wait_ge(w_ternary, 2)
                    for t in range(TB):
                        if t % 2 == 0:
                            wait(pe, h_ready, it, 2 * FT, FT * (u + 1))
                            wait(pe, hl_ready, it, 2 * FT, FT * (u + 1))
                        n = 0
                        for hid in (hh, hl):
                            for f in range(FT):
                                mm = nc.tensor.matmul(ps[:, t // 2, t % 2 * D:(t % 2 + 1) * D],
                                                      hid[:, f, t * P:(t + 1) * P], w2q[:, f, :],
                                                      start=(n == 0), stop=(n == 2 * FT - 1))
                                n += 1
                        if t % 2:
                            mm.then_inc(y_mm, 1)

            looped(pe, B, {2, 2 * DH, 2 * FT, TB, 2 * TB, 2 * MT}, body)


def part_b(nc, qk_d, v_d, out, Y, ident):
    with ExitStack() as ctx:
        def sb(name, shape, dt=F32):
            return ctx.enter_context(nc.sbuf_tensor(name, shape, dt))

        def sem(name):
            return ctx.enter_context(nc.semaphore(name))

        sc = ctx.enter_context(nc.psum_tensor("ps_scores", [P, NS, BANK], F32))
        mx = ctx.enter_context(nc.psum_tensor("ps_maxima", [P, NS, BANK], F32))
        po = ctx.enter_context(nc.psum_tensor("ps_out", [P, BANK], F32))
        pt = ctx.enter_context(nc.psum_tensor("ps_turn", [P, BANK], F32))
        qs = sb("q_stack", [P, UN, 2, S], F32R)
        ks = sb("k_stack", [P, UN, 2, S], F32R)
        vt = sb("v_tile", [P, UN, NT, 2 * VC])
        pr = sb("probs", [P, NP, 4, BANK])
        mpart = sb("max_halves", [P, 2, SLOTS])
        mcol = sb("max_cols", [P, SLOTS // 2])
        mhi = sb("max_hi", [2 * NT, P], F32R)
        mlo = sb("max_lo", [2 * NT, P], F32R)
        osb = sb("o_t", [P, BANK])
        rec = sb("rec", [P, 2 * NT])
        on = sb("o_norm", [P, 2 * NT, HD])

        ones_set = sem("ones_set")
        zeros_set = sem("zeros_set")
        zeros_set_pool = sem("zeros_set_pool")
        out_zeroed = sem("out_zeroed")
        first_loaded = sem("first_loaded")
        loaded = [sem(f"loaded{r}") for r in range(UN)]
        scores_mm = sem("scores_mm")
        probs_ready = sem("probs_ready")
        max_mm = sem("max_mm")
        max_taken = sem("max_taken")
        cols_ready = sem("cols_ready")
        cols_turned = sem("cols_turned")
        row_hi_ready = sem("row_hi_ready")
        row_lo_ready = sem("row_lo_ready")
        rows_placed = [sem("rows_placed0"), sem("rows_placed1")]
        pv_mm = sem("pv_mm")
        o_copied = sem("o_copied")
        o_turned = sem("o_turned")
        rec_ready = sem("rec_ready")
        o_normed = sem("o_normed")
        y_added = sem("y_added")
        y_stored = sem("y_stored")

        def waitp(eng, s, it, j, per, add):
            wait(eng, s, it, UN * per, per * j + add)

        def ring(j, s, start):
            k = (j * SLOTS + s - start) % (UN * SLOTS)
            return k % NS, NS if k >= NS else k + UN * SLOTS - ((UN * SLOTS - 1 - k) // NS * NS + k)

        def score_bank(j, s):
            return ring(j, s, SCORE_START)[0]

        def max_bank(j, s):
            return ring(j, s, MAX_START)[0]

        def lead(t):
            return (1, t + LEAD) if t + LEAD < STEPS else (2, t + LEAD - STEPS)

        TURN = STEPS - LEAD

        O_STEP = 1

        block = ctx.enter_context(nc.Block())

        @block.sync
        def _(sp):
            def load_stacks(pair, r, a, done):
                for qk, st in ((0, qs), (1, ks)):
                    two = qk_d[qk, bass.ds(2 * pair + a, 1)][0]
                    src = two[0].unsqueeze(0).broadcast_to([2, HD, S]) if qk == 0 else two
                    sp.dma_start(st[0:2 * HD, r, a, :].bitcast(F32), src).then_inc(done, 16)
                    sp.dma_start(st[2 * HD:QROWS, r, a, :].bitcast(F32), two[1 - qk]).then_inc(done, 16)

            def load_v(pair, r):
                sp.dma_start(vt[:, r], v_d[bass.ds(pair, 1)][0]).then_inc(loaded[r], 16)

            def place(it, j, r, parity):
                waitp(sp, row_lo_ready, it, j, 1, 1)
                for a in range(2):
                    for n, part in enumerate((mhi, mlo)):
                        row = MROW + n
                        sp.dma_start(qs[row:row + 1, r, a, :].bitcast(F32),
                                     part[a * NT:(a + 1) * NT, :].bitcast(F32)).then_inc(rows_placed[parity], 16)

            for r in range(UN - 1):
                for a in range(2):
                    sp.wait_ge(ones_set, 2 * r + a + 1)
                    if r == 0:
                        sp.wait_ge(zeros_set, a + 1)
                    elif a == 0:
                        sp.wait_ge(zeros_set_pool, r)
                    load_stacks(r, r, a, first_loaded if r == a == 0 else loaded[r])
                load_v(r, r)
            place(0, 0, 0, 0)
            sp.wait_ge(ones_set, 2 * UN)
            sp.wait_ge(zeros_set_pool, UN - 1)

            def body(it, first, last):
                for j in range(UN):
                    if not (last and j > 0):
                        pair = UN * at(it) + j + 3
                        if not isinstance(it, int):
                            pair = sp.snap(pair)
                        wait_all(sp, (scores_mm, it, UN * SLOTS, SLOTS * j), (pv_mm, it, UN * STEPS, STEPS * j))
                        for a in range(2):
                            load_stacks(pair, (j + 3) % UN, a, loaded[(j + 3) % UN])
                        load_v(pair, (j + 3) % UN)
                    if not (last and j == UN - 1):
                        place(it, j + 1, (j + 1) % UN, (j + 1) % 2)

            looped(sp, NIT, {UN, UN * SLOTS, UN * STEPS}, body)

        @block.gpsimd
        def _(pool):
            for r in range(UN):
                for a in range(2):
                    nc.gpsimd.memset(ks[:, r, a].bitcast(F32), 1.0).then_inc(ones_set, 1)
                if r:
                    nc.gpsimd.memset(qs[:, r].bitcast(F32), 0.0).then_inc(zeros_set_pool, 1)

            def body(b, first, last):
                for g in range(2):
                    for j in range(UN):
                        wait(pool, o_normed, b, 2 * UN, UN * g + j + 1)
                        yv = Y[:, bass.ds(2 * at(b) + g, 1), :, j * 2 * HD:(j + 1) * 2 * HD].rearrange(
                            "p o (q t) c -> p t (o q) c", q=2)
                        nc.gpsimd.tensor_tensor(yv, yv, on[:].rearrange("p (t q a) c -> p t q (a c)", q=2, a=2),
                                                ALU.add).then_inc(y_added, 1)
                    wait(pool, y_added, b, 2 * UN, UN * (g + 1))
                    pool.dma_start(out[bass.ds(at(b), 1), :, g * P:(g + 1) * P].rearrange(
                        "o (t p) c -> p (o t) c", p=P), Y[:, bass.ds(2 * at(b) + g, 1)].rearrange(
                        "p o t c -> p (o t) c")).then_inc(y_stored, 16)

            looped(pool, B, {2 * UN}, body)
            pool.wait_ge(y_stored, 16 * NIT)

        @block.scalar
        def _(act):
            def exps(it, j, t, slots):
                for s in slots:
                    waitp(act, scores_mm, it, j, SLOTS, 4 * t + s + 1)
                    if s == 0:
                        waitp(act, pv_mm, it, j, STEPS, t - NP + 1)
                    nc.scalar.activation(pr[:, t % NP, s, :], sc[:, score_bank(j, 4 * t + s), :], ACT.Exp,
                                         scale=1.0 / D ** 0.5).then_inc(probs_ready, 1)

            def row_hi(it, j):
                waitp(act, cols_turned, it, j, 1, 1)
                waitp(act, row_lo_ready, it, j, 1, 0)
                wait(act, rows_placed[(j - 1) % 2], it, 32 * UN, 64 * ((j - 1) // 2 + 1))
                nc.scalar.activation(mhi[:], pt[0:2 * NT, 0:P], ACT.Copy, scale=-1.0).then_inc(row_hi_ready, 1)

            def copy_o(it, j):
                waitp(act, pv_mm, it, j, STEPS, STEPS)
                waitp(act, o_turned, it, j, 1, 0)
                nc.scalar.activation(osb[:], po[:], ACT.Copy).then_inc(o_copied, 1)

            row_hi(0, 0)

            def body(it, first, last):
                for j in range(UN):
                    for t in range(STEPS):
                        exps(it, j, t, (0, 1))
                        if t == 0 and not (first and j == 0):
                            copy_o(it, j - 1)
                        exps(it, j, t, (2, 3))
                        if t == TURN and not (last and j == UN - 1):
                            row_hi(it, j + 1)

            looped(act, NIT, {UN, UN * SLOTS, UN * STEPS, 32 * UN}, body)
            copy_o(NIT - 1, UN - 1)

        @block.vector
        def _(dve):
            for a in range(2):
                nc.vector.memset(qs[:, 0, a].bitcast(F32), 0.0).then_inc(zeros_set, 1)
            nc.vector.memset(po[:], 0.0).then_inc(out_zeroed, 1)

            def maxima(it, j, g, half):
                for s in range(4 * g + 2 * half, 4 * g + 2 * half + 2):
                    waitp(dve, max_mm, it, j, SLOTS, s + 1)
                    nc.vector.tensor_reduce(mpart[:, j % 2, s:s + 1], mx[:, max_bank(j, s), :], AX_X,
                                            ALU.max).then_inc(max_taken, 1)

            def join(it, j):
                waitp(dve, max_taken, it, j, SLOTS, SLOTS)
                waitp(dve, cols_turned, it, j, 1, 0)
                nc.vector.tensor_reduce(mcol[:], mpart[:, j % 2, :].rearrange("p (n k) -> p n k", k=2), AX_X,
                                        ALU.max).then_inc(cols_ready, 1)

            def row_lo(it, j):
                waitp(dve, row_hi_ready, it, j, 1, 1)
                nc.vector.scalar_tensor_tensor(mlo[:], pt[0:2 * NT, 0:P], -1.0, mhi[:].bitcast(F32), ALU.mult,
                                               ALU.subtract).then_inc(row_lo_ready, 1)

            turned = pt[:].rearrange("p (n c) -> p n c", c=32)

            def reciprocal(it, j):
                waitp(dve, o_turned, it, j, 1, 1)
                nc.vector.reciprocal(rec[:], turned[:, :, HD]).then_inc(rec_ready, 1)

            def norm_o(it, j):
                waitp(dve, rec_ready, it, j, 1, 1)
                waitp(dve, y_added, it, j, 1, 0)
                nc.vector.tensor_tensor(on[:], turned[:, :, 0:HD],
                                        rec[:].unsqueeze(2).broadcast_to([P, 2 * NT, HD]),
                                        ALU.mult).then_inc(o_normed, 1)

            for g in range(STEPS):
                for half in range(2):
                    maxima(0, 0, g, half)
            join(0, 0)
            row_lo(0, 0)
            for g in range(LEAD):
                for half in range(2):
                    maxima(0, 1, g, half)

            def body(it, first, last):
                for j in range(UN):
                    for t in range(STEPS):
                        ahead, g = lead(t)
                        maxing = not (last and j + ahead >= UN)
                        if maxing:
                            maxima(it, j + ahead, g, 0)
                        if t == O_STEP + 1 and not (first and j == 0):
                            reciprocal(it, j - 1)
                        if t == O_STEP + 2 and not (first and j == 0):
                            norm_o(it, j - 1)
                        if t == TURN and not (last and j == UN - 1):
                            join(it, j + 1)
                        if t == TURN + 1 and not (last and j == UN - 1):
                            row_lo(it, j + 1)
                        if maxing:
                            maxima(it, j + ahead, g, 1)

            looped(dve, NIT, {UN, UN * SLOTS}, body)
            reciprocal(NIT - 1, UN - 1)
            norm_o(NIT - 1, UN - 1)

        @block.tensor
        def _(pe):
            def max_slot(it, j, s):
                r = j % UN
                a, qt, kh = s // (2 * NT), s // 2 % NT, s % 2
                if isinstance(it, int) and it == j == 0:
                    if s == 0:
                        pe.wait_ge(first_loaded, 64)
                    elif s == 2 * NT:
                        pe.wait_ge(loaded[r], LOADS - 64)
                elif s == 0:
                    wait(pe, loaded[r], it, LOADS, LOADS * (j // UN + 1) - (64 if r == 0 else 0))
                waitp(pe, max_taken, it, j, SLOTS, s + 1 - ring(j, s, MAX_START)[1])
                nc.tensor.matmul(mx[:, max_bank(j, s), :], qs[0:MROW, r, a, qt * P:(qt + 1) * P],
                                 ks[0:MROW, r, a, kh * BANK:(kh + 1) * BANK],
                                 start=True, stop=True).then_inc(max_mm, 1)

            def score_slot(it, j, s):
                r = j % UN
                kt, a, qh = s // 4, s // 2 % 2, s % 2
                if s == 0:
                    wait(pe, rows_placed[j % 2], it, 32 * UN, 64 * (j // 2 + 1))
                waitp(pe, probs_ready, it, j, SLOTS, s + 1 - ring(j, s, SCORE_START)[1])
                nc.tensor.matmul(sc[:, score_bank(j, s), :], ks[0:CR, r, a, kt * P:(kt + 1) * P],
                                 qs[0:CR, r, a, qh * BANK:(qh + 1) * BANK],
                                 start=True, stop=True).then_inc(scores_mm, 1)

            def products(it, j, t):
                r = j % UN
                waitp(pe, probs_ready, it, j, SLOTS, 4 * t + 4)
                if t == 0:
                    waitp(pe, o_copied, it, j, 1, 0)
                for g in range(4):
                    qh, a = g // 2, g % 2
                    mm = nc.tensor.matmul(po[32 * g:32 * g + VC, :], vt[:, r, t, a * VC:(a + 1) * VC],
                                          pr[:, t % NP, 2 * a + qh, :], start=(t == 0),
                                          stop=(t == STEPS - 1))
                mm.then_inc(pv_mm, 1)

            def turn_cols(it, j):
                waitp(pe, cols_ready, it, j, 1, 1)
                waitp(pe, o_normed, it, j, 1, -1)
                nc.tensor.transpose(pt[0:2 * NT, 0:P], mcol[:], ident[:]).then_inc(cols_turned, 1)

            def turn_o(it, j, final=False):
                waitp(pe, o_copied, it, j, 1, 1)
                if final:
                    waitp(pe, o_normed, it, j, 1, 0)
                else:
                    waitp(pe, row_lo_ready, it, j, 1, 2)
                for n in range(4):
                    mm = nc.tensor.transpose(pt[:, n * P:(n + 1) * P], osb[:, n * P:(n + 1) * P], ident[:])
                mm.then_inc(o_turned, 1)

            for s in range(SLOTS):
                max_slot(0, 0, s)
            pe.wait_ge(out_zeroed, 1)
            for s in range(4 * LEAD):
                max_slot(0, 1, s)
                if s == 1:
                    turn_cols(0, 0)

            def body(it, first, last):
                for j in range(UN):
                    for t in range(STEPS):
                        ahead, g = lead(t)
                        maxing = not (last and j + ahead >= UN)
                        for n in range(4):
                            score_slot(it, j, 4 * t + n)
                            if maxing:
                                max_slot(it, j + ahead, 4 * g + n)
                            if n == 3 and t == TURN and not (last and j == UN - 1):
                                turn_cols(it, j + 1)
                            if n == 1:
                                if t:
                                    products(it, j, t - 1)
                                elif not (first and j == 0):
                                    products(it, j - 1, STEPS - 1)
                        if t == O_STEP and not (first and j == 0):
                            turn_o(it, j - 1)

            looped(pe, NIT, {UN, UN * SLOTS, LOADS, 32 * UN}, body)
            products(NIT - 1, UN - 1, STEPS - 1)
            turn_o(NIT - 1, UN - 1, final=True)


def program(nc, x, wqkt, wvt, w1t, w2t, b1t, b2, out):
    qk_d = nc.dram_tensor("qk_parts", [2, B * H, 2, HD, S], F32, kind="Internal").ap()
    v_d = nc.dram_tensor("v_pairs", [PAIRS, P, NT, 2 * VC], F32, kind="Internal").ap()
    with ExitStack() as ctx:
        Y = ctx.enter_context(nc.sbuf_tensor("Y", [P, DH * B, NT, P], F32))
        ident = ctx.enter_context(nc.sbuf_tensor("ident", [P, P], F32))
        part_a(nc, x, wqkt, wvt, w1t, w2t, b1t, b2, qk_d, v_d, Y, ident)
        part_b(nc, qk_d, v_d, out, Y, ident)


def kernel(**inputs):
    import numpy as np
    import concourse.bacc as bacc
    from concourse.bass_utils import run_bass_kernel_spmd

    w = {n: np.asarray(inputs[f"L0_{n}"]) for n in ("attn_Wq", "attn_Wk", "attn_Wv", "ffn_W1", "ffn_W2",
                                                    "ffn_b1", "ffn_b2")}
    arrays = {
        "x": np.asarray(inputs["L0_attn_x"]),
        "wqkt": np.concatenate([w["attn_Wq"].T, w["attn_Wk"].T], axis=1),
        "wvt": w["attn_Wv"].T,
        "w1t": w["ffn_W1"].T,
        "w2t": w["ffn_W2"].T,
        "b1t": w["ffn_b1"].reshape(FT, P).T,
        "b2": w["ffn_b2"],
    }
    arrays = {n: np.ascontiguousarray(a) for n, a in arrays.items()}
    nc = bacc.Bacc("TRN2", target_bir_lowering=False, num_devices=1)
    args = [nc.dram_tensor(n, a.shape, F32, kind="ExternalInput").ap() for n, a in arrays.items()]
    out = nc.dram_tensor("out", (B, S, D), F32, kind="ExternalOutput").ap()
    program(nc, *args, out)
    r = run_bass_kernel_spmd(nc, [arrays], core_ids=[0])
    return r.results[0]["out"]
```
